# Optimizing a Trainium2 kernel written in Bass

```python
import numpy as np
import jax
import jax.numpy as jnp

def _softmax(x, axis=-1):
    return jax.nn.softmax(x, axis=axis)

def _gelu(x):
    return jax.nn.gelu(x, approximate=True)

def _silu(x):
    return jax.nn.silu(x)

def _sigmoid(x):
    return jax.nn.sigmoid(x)

def _layernorm(x, axis=-1, eps=1e-05):
    m = jnp.mean(x, axis=axis, keepdims=True)
    v = jnp.var(x, axis=axis, keepdims=True)
    return (x - m) / jnp.sqrt(v + eps)

def _scatter_add(tgt, idx, src, axis=0):
    return tgt.at[idx].add(src)

def _segment_sum(src, seg, n):
    return jax.ops.segment_sum(src, seg, n)
kernel_name = 'mk_dlrm_tower_d1_rec_r8_4f7285'

def setup_inputs(seed: int=0):
    np.random.seed(seed)
    _w = jnp.asarray

    def _rec_inputs():
        import jax
        import jax.numpy as jnp
        _tk = jax.random.key(seed)
        ids = jnp.stack([jax.random.randint(jax.random.fold_in(_tk, 200 + f), (2048,), 0, v, jnp.int32) for f, v in enumerate([1250, 125000, 1250, 1000, 1250, 1000, 1250, 1250, 1250, 1250, 1000, 1250, 1000, 12500, 1250, 1000, 1000, 1250, 1000, 12500, 12500, 1250, 1250, 12500, 12500, 12500])], axis=1)
        tbl_0 = 0.05 * jax.random.normal(jax.random.fold_in(_tk, 500 + 0), (1250, 128), jnp.float32)
        tbl_1 = 0.05 * jax.random.normal(jax.random.fold_in(_tk, 500 + 1), (125000, 128), jnp.float32)
        tbl_2 = 0.05 * jax.random.normal(jax.random.fold_in(_tk, 500 + 2), (1250, 128), jnp.float32)
        tbl_3 = 0.05 * jax.random.normal(jax.random.fold_in(_tk, 500 + 3), (1000, 128), jnp.float32)
        tbl_4 = 0.05 * jax.random.normal(jax.random.fold_in(_tk, 500 + 4), (1250, 128), jnp.float32)
        tbl_5 = 0.05 * jax.random.normal(jax.random.fold_in(_tk, 500 + 5), (1000, 128), jnp.float32)
        tbl_6 = 0.05 * jax.random.normal(jax.random.fold_in(_tk, 500 + 6), (1250, 128), jnp.float32)
        tbl_7 = 0.05 * jax.random.normal(jax.random.fold_in(_tk, 500 + 7), (1250, 128), jnp.float32)
        tbl_8 = 0.05 * jax.random.normal(jax.random.fold_in(_tk, 500 + 8), (1250, 128), jnp.float32)
        tbl_9 = 0.05 * jax.random.normal(jax.random.fold_in(_tk, 500 + 9), (1250, 128), jnp.float32)
        tbl_10 = 0.05 * jax.random.normal(jax.random.fold_in(_tk, 500 + 10), (1000, 128), jnp.float32)
        tbl_11 = 0.05 * jax.random.normal(jax.random.fold_in(_tk, 500 + 11), (1250, 128), jnp.float32)
        tbl_12 = 0.05 * jax.random.normal(jax.random.fold_in(_tk, 500 + 12), (1000, 128), jnp.float32)
        tbl_13 = 0.05 * jax.random.normal(jax.random.fold_in(_tk, 500 + 13), (12500, 128), jnp.float32)
        tbl_14 = 0.05 * jax.random.normal(jax.random.fold_in(_tk, 500 + 14), (1250, 128), jnp.float32)
        tbl_15 = 0.05 * jax.random.normal(jax.random.fold_in(_tk, 500 + 15), (1000, 128), jnp.float32)
        tbl_16 = 0.05 * jax.random.normal(jax.random.fold_in(_tk, 500 + 16), (1000, 128), jnp.float32)
        tbl_17 = 0.05 * jax.random.normal(jax.random.fold_in(_tk, 500 + 17), (1250, 128), jnp.float32)
        tbl_18 = 0.05 * jax.random.normal(jax.random.fold_in(_tk, 500 + 18), (1000, 128), jnp.float32)
        tbl_19 = 0.05 * jax.random.normal(jax.random.fold_in(_tk, 500 + 19), (12500, 128), jnp.float32)
        tbl_20 = 0.05 * jax.random.normal(jax.random.fold_in(_tk, 500 + 20), (12500, 128), jnp.float32)
        tbl_21 = 0.05 * jax.random.normal(jax.random.fold_in(_tk, 500 + 21), (1250, 128), jnp.float32)
        tbl_22 = 0.05 * jax.random.normal(jax.random.fold_in(_tk, 500 + 22), (1250, 128), jnp.float32)
        tbl_23 = 0.05 * jax.random.normal(jax.random.fold_in(_tk, 500 + 23), (12500, 128), jnp.float32)
        tbl_24 = 0.05 * jax.random.normal(jax.random.fold_in(_tk, 500 + 24), (12500, 128), jnp.float32)
        tbl_25 = 0.05 * jax.random.normal(jax.random.fold_in(_tk, 500 + 25), (12500, 128), jnp.float32)
        _rk = jax.random.fold_in(_tk, 7)
        r_dense_features = -0.000520686 + 1.00062 * jax.random.normal(jax.random.fold_in(_rk, 101), (2048, 128), jnp.float32)
        W_top1 = 0.0405887 * jax.random.normal(jax.random.fold_in(_tk, 801), (607, 512), jnp.float32)
        W_top2 = 0.0441942 * jax.random.normal(jax.random.fold_in(_tk, 802), (512, 256), jnp.float32)
        W_top3 = 0.0625 * jax.random.normal(jax.random.fold_in(_tk, 803), (256, 1), jnp.float32)
        b_top1 = jnp.zeros((512,), jnp.float32)
        b_top2 = jnp.zeros((256,), jnp.float32)
        return (r_dense_features, ids, tbl_0, tbl_1, tbl_2, tbl_3, tbl_4, tbl_5, tbl_6, tbl_7, tbl_8, tbl_9, tbl_10, tbl_11, tbl_12, tbl_13, tbl_14, tbl_15, tbl_16, tbl_17, tbl_18, tbl_19, tbl_20, tbl_21, tbl_22, tbl_23, tbl_24, tbl_25, W_top1, b_top1, W_top2, b_top2, W_top3)
    r_dense_features, ids, tbl_0, tbl_1, tbl_2, tbl_3, tbl_4, tbl_5, tbl_6, tbl_7, tbl_8, tbl_9, tbl_10, tbl_11, tbl_12, tbl_13, tbl_14, tbl_15, tbl_16, tbl_17, tbl_18, tbl_19, tbl_20, tbl_21, tbl_22, tbl_23, tbl_24, tbl_25, W_top1, b_top1, W_top2, b_top2, W_top3 = _rec_inputs()

    def _L0_rec_setup():
        import jax, jax.numpy as jnp
        import numpy as np
        F = 26
        N = F + 1
        _TRIU_I, _TRIU_J = np.triu_indices(N, k=1)
        key = jax.random.key(seed)
        k1, k2 = jax.random.split(key)
        B, D = (2048, 128)
        dense_features = jax.random.normal(k1, (B, D), dtype=jnp.float32)
        sparse_features = jax.random.normal(k2, (B, F, D), dtype=jnp.float32)
        return {'dense_features': dense_features, 'sparse_features': sparse_features}
    _L0_rec_all = _L0_rec_setup()
    _L0_rec_in = {k: v for k, v in _L0_rec_all.items() if k in ()}
    del _L0_rec_all
    return {'r_dense_features': r_dense_features, 'ids': ids, 'tbl_0': tbl_0, 'tbl_1': tbl_1, 'tbl_2': tbl_2, 'tbl_3': tbl_3, 'tbl_4': tbl_4, 'tbl_5': tbl_5, 'tbl_6': tbl_6, 'tbl_7': tbl_7, 'tbl_8': tbl_8, 'tbl_9': tbl_9, 'tbl_10': tbl_10, 'tbl_11': tbl_11, 'tbl_12': tbl_12, 'tbl_13': tbl_13, 'tbl_14': tbl_14, 'tbl_15': tbl_15, 'tbl_16': tbl_16, 'tbl_17': tbl_17, 'tbl_18': tbl_18, 'tbl_19': tbl_19, 'tbl_20': tbl_20, 'tbl_21': tbl_21, 'tbl_22': tbl_22, 'tbl_23': tbl_23, 'tbl_24': tbl_24, 'tbl_25': tbl_25, 'W_top1': W_top1, 'b_top1': b_top1, 'W_top2': W_top2, 'b_top2': b_top2, 'W_top3': W_top3}

def reference(r_dense_features, ids, tbl_0, tbl_1, tbl_2, tbl_3, tbl_4, tbl_5, tbl_6, tbl_7, tbl_8, tbl_9, tbl_10, tbl_11, tbl_12, tbl_13, tbl_14, tbl_15, tbl_16, tbl_17, tbl_18, tbl_19, tbl_20, tbl_21, tbl_22, tbl_23, tbl_24, tbl_25, W_top1, b_top1, W_top2, b_top2, W_top3):
    import jax
    import jax.numpy as jnp

    def _L0_rec_ref(dense_features, sparse_features):
        import jax, jax.numpy as jnp
        import numpy as np
        F = 26
        N = F + 1
        _TRIU_I, _TRIU_J = np.triu_indices(N, k=1)
        combined = jnp.concatenate([dense_features[:, None, :], sparse_features], axis=1)
        interactions = jnp.einsum('bnd,bmd->bnm', combined, combined)
        interactions_flat = interactions[:, _TRIU_I, _TRIU_J]
        return jnp.concatenate([dense_features, interactions_flat], axis=1)
    e = jnp.stack([tbl_0[ids[:, 0]], tbl_1[ids[:, 1]], tbl_2[ids[:, 2]], tbl_3[ids[:, 3]], tbl_4[ids[:, 4]], tbl_5[ids[:, 5]], tbl_6[ids[:, 6]], tbl_7[ids[:, 7]], tbl_8[ids[:, 8]], tbl_9[ids[:, 9]], tbl_10[ids[:, 10]], tbl_11[ids[:, 11]], tbl_12[ids[:, 12]], tbl_13[ids[:, 13]], tbl_14[ids[:, 14]], tbl_15[ids[:, 15]], tbl_16[ids[:, 16]], tbl_17[ids[:, 17]], tbl_18[ids[:, 18]], tbl_19[ids[:, 19]], tbl_20[ids[:, 20]], tbl_21[ids[:, 21]], tbl_22[ids[:, 22]], tbl_23[ids[:, 23]], tbl_24[ids[:, 24]], tbl_25[ids[:, 25]]], axis=1)
    z = _L0_rec_ref(r_dense_features, e)
    z = z.reshape(z.shape[0], -1)
    h = jnp.concatenate([z, r_dense_features], axis=1)
    h = jnp.maximum(h @ W_top1 + b_top1, 0.0)
    h = jnp.maximum(h @ W_top2 + b_top2, 0.0)
    y = h @ W_top3
    return y

_drawn_inputs = setup_inputs


def setup_inputs(seed=0):
    import zlib

    import numpy as np

    out = dict(_drawn_inputs(seed))
    spreads = {'b_top1': (0.0, 0.1), 'b_top2': (0.0, 0.1)}
    factors = {}
    for name, (base, spread) in spreads.items():
        noise = np.random.default_rng([zlib.crc32(name.encode()), seed]).standard_normal(out[name].shape)
        drawn = base * np.exp(spread * noise) if base else spread * noise
        out[name] = jnp.asarray(drawn.astype(out[name].dtype))
    for name, factor in factors.items():
        out[name] = (out[name] * factor).astype(out[name].dtype)
    return out
```

```python
import concourse.bass as bass
from concourse import mybir
from contextlib import ExitStack

P = 128
QUAD = 32


def dlrm_tower_kernel(nc, dense, ids, tables, W1, b1, W2, b2, W3, y):
    fp32 = mybir.dt.float32
    ALU = mybir.AluOpType
    ACT = mybir.ActivationFunctionType

    B, D = dense.shape
    F = len(tables)
    N = F + 1
    H1, H2 = W2.shape
    TILES = B // P
    PAIR_ROWS = N * (N - 1) // 2
    GROUP = 4
    GROUPS = -(-N // GROUP)
    LANES = P // QUAD
    MQ = -(-(N - 1) // LANES)
    UNITS = 4
    UG = P // LANES // UNITS
    BANK = 512
    GB = BANK // P
    HC1, HC2 = H1 // P, H2 // P

    def columns(q):
        return min(MQ, N - 1 - MQ * q)

    def rows_of_chunk(mm):
        return QUAD * sum(mm < columns(q) for q in range(LANES))

    def pair_row(n, m):
        return D + n * (2 * N - n - 1) // 2 + (m - n - 1)

    def group_size(k):
        return min(GROUP, N - GROUP * k)

    pair_runs = []
    for n in range(N - 1):
        for q in range(LANES):
            lo = max(0, n - MQ * q)
            if lo < columns(q):
                pair_runs.append((n, lo, columns(q), q))

    ctx = ExitStack()
    with ctx:
        def sb(name, shape, dt=fp32):
            return ctx.enter_context(nc.sbuf_tensor(name, shape, dt))

        def pb(name, shape):
            return ctx.enter_context(nc.psum_tensor(name, shape, fp32))

        def sem(name):
            return ctx.enter_context(nc.semaphore(name))

        idx = sb("idx", [P, 2, F], mybir.dt.int32)
        ident = sb("ident", [P, P])
        w_dense = sb("w_dense", [D, H1])
        w_dense2 = sb("w_dense2", [D, H1])
        w_pair = sb("w_pair", [P, MQ, H1])
        w2_sb = sb("w2_sb", [P, HC1, H2])
        w3_sb = sb("w3_sb", [P, HC2])
        b1_sb = sb("b1_sb", [P, HC1])
        b2_sb = sb("b2_sb", [P, HC2])
        emb = sb("emb", [P, 2, N, D])
        featT = sb("featT", [D, 2, P, QUAD])
        denseT = sb("denseT", [D, 2, P])
        pairs = sb("pairs", [P, 2, MQ, P])
        h1 = sb("h1", [P, 2, HC1, P])
        h2 = sb("h2", [P, 2, HC2, P])
        y_sb = sb("y_sb", [P, TILES])

        ps_t = pb("ps_t", [P, 2, GROUP, P])
        ps_g = pb("ps_g", [P, 2, UG, P])
        ps_m = pb("ps_m", [P, 2, BANK])

        s_wd, s_wp, s_w2 = (sem(n) for n in ("s_wd", "s_wp", "s_w2"))
        s_gather = [[sem(f"s_gather{b}_{k}") for k in range(GROUPS)] for b in range(2)]
        s_idx = [sem(f"s_idx{b}") for b in range(2)]
        s_dense = [sem(f"s_dense{b}") for b in range(2)]
        s_open = sem("s_open")
        s_out = sem("s_out")
        s_ident0, s_ident, s_zero, s_zero_feat, s_wsum = (
            sem(n) for n in ("s_ident0", "s_ident", "s_zero", "s_zero_feat", "s_wsum"))
        s_tr, s_gram, s_p1, s_p2, s_py = (sem(n) for n in ("s_tr", "s_gram", "s_p1", "s_p2", "s_py"))
        s_tr_v, s_tr_a, s_dt = sem("s_tr_v"), sem("s_tr_a"), sem("s_dt")
        s_gram_v, s_gram_a = sem("s_gram_v"), sem("s_gram_a")
        s_h1_v, s_h1_a, s_h2_v, s_h2_a, s_y = (
            sem(n) for n in ("s_h1_v", "s_h1_a", "s_h2_v", "s_h2_a", "s_y"))

        block = ctx.enter_context(nc.Block())

        dense_t = dense.rearrange("(p t) d -> t p d", t=TILES)
        ids_t = ids.rearrange("(p t) f -> t p f", t=TILES)

        def unit_move(b, u, j, q):
            c = columns(q)
            m0 = (N - 1) * j + MQ * q
            s0 = u * UG * LANES + j
            return (pairs[QUAD * q:QUAD * (q + 1), b, 0:c, s0:s0 + LANES * (UG - 1) + 1:LANES]
                    .rearrange("p m g -> p g m"),
                    ps_g[QUAD * j:QUAD * (j + 1), u % 2, :, m0:m0 + c])

        def both_tiles(eng, tile):
            for b in range(2):
                tile(0, b, True)
            with eng.Fori(1, TILES // 2) as i:
                for b in range(2):
                    tile(i, b, False)

        @block.sync
        def _(sp):
            def load_tile(i, b):
                sp.dma_start(idx[:, b, :], ids_t[2 * i + b]).then_inc(s_idx[b], 16)
                sp.dma_start(emb[:, b, 0, :], dense_t[2 * i + b]).then_inc(s_dense[b], 16)

            for b in range(2):
                load_tile(0, b)
            sp.dma_start(w_dense[:], W1[0:D, :]).then_inc(s_wd, 16)
            sp.dma_start(w_dense2[:], W1[D + PAIR_ROWS:D + PAIR_ROWS + D, :]).then_inc(s_wd, 16)
            sp.dma_start(w2_sb[:], W2.rearrange("(c p) n -> p c n", p=P)).then_inc(s_w2, 16)
            with nc.allow_non_contiguous_dma(reason="bias and last-layer vectors, 4 bytes a partition"):
                sp.dma_start(b1_sb[:], b1.rearrange("(c p) -> p c", p=P)).then_inc(s_w2, 16)
                sp.dma_start(b2_sb[:], b2.rearrange("(c p) -> p c", p=P)).then_inc(s_w2, 16)
                sp.dma_start(w3_sb[:], W3.rearrange("(c p) o -> p (c o)", p=P)).then_inc(s_w2, 16)
            sp.wait_ge(s_zero, 1)
            for n, lo, hi, q in pair_runs:
                r = pair_row(n, 1 + MQ * q + lo)
                part = QUAD * q + n
                sp.dma_start(w_pair[part:part + 1, lo:hi, :],
                             W1[r:r + hi - lo, :].rearrange("(a r) h -> a r h", a=1)).then_inc(s_wp, 16)
            with sp.Fori(1, TILES // 2) as i:
                for b in range(2):
                    sp.wait_ge(s_tr, (2 * i + b - 1) * GROUPS)
                    load_tile(i, b)
            sp.wait_ge(s_y, TILES)
            sp.dma_start(y.rearrange("(p t) o -> p (t o)", t=TILES), y_sb[:]).then_inc(s_out, 16)
            sp.wait_ge(s_out, 16)

        @block.gpsimd
        def _(pool):
            def tile(i, b, first):
                t = 2 * i + b
                pool.wait_ge(s_idx[b], 16 * (i + 1))
                pool.sem_inc(s_open, 1)
                for k in range(GROUPS):
                    for n in range(max(1, GROUP * k), GROUP * k + group_size(k)):
                        pool.indirect_dma_start(
                            emb[:, b, n, :], None, tables[n - 1][:, :],
                            bass.IndirectOffsetOnAxis(ap=idx[:, b, n - 1:n], axis=0),
                        ).then_inc(s_gather[b][k], 16)

            pool.wait_ge(s_ident0, 1)
            pool.affine_select(out=ident[:], in_=ident[:], compare_op=ALU.not_equal, fill=1.0, base=0,
                               pattern=[[-1, P]], channel_multiplier=1).then_inc(s_ident, 1)
            both_tiles(pool, tile)

        @block.vector
        def _(dve):
            nc.vector.memset(w_pair[:], 0.0).then_inc(s_zero, 1)
            nc.vector.memset(featT[:, :, :, N:QUAD], 0.0).then_inc(s_zero_feat, 1)
            nc.vector.memset(ident[:], 0.0).then_inc(s_ident0, 1)
            dve.wait_ge(s_wd, 32)
            nc.vector.tensor_tensor(w_dense[:], w_dense[:], w_dense2[:], ALU.add).then_inc(s_wsum, 1)
            dve.wait_ge(s_w2, 64)

            def tile(i, b, first):
                t = 2 * i + b
                for k in range(GROUPS):
                    if (GROUPS * b + k) % 2 == 0:
                        if not first:
                            dve.wait_ge(s_p1, HC1 * (t - 1))
                        dve.wait_ge(s_tr, t * GROUPS + k + 1)
                        if k == 0:
                            nc.vector.tensor_copy(denseT[:, b, :], ps_t[:, GROUPS * b % 2, 0, :]).then_inc(s_dt, 1)
                        g = group_size(k)
                        nc.vector.tensor_copy(
                            featT[:, b, :, GROUP * k:GROUP * k + g].rearrange("p s f -> p f s"),
                            ps_t[:, (GROUPS * b + k) % 2, 0:g, :]).then_inc(s_tr_v, 1)
                for u in range(UNITS):
                    dve.wait_ge(s_gram, t * UNITS + u + 1)
                    for j in (0, 1):
                        for q in range(LANES):
                            nc.vector.tensor_copy(*unit_move(b, u, j, q)).then_inc(s_gram_v, 1)
                for c in range(1, HC1, 2):
                    dve.wait_ge(s_p1, HC1 * t + c + 1)
                    if not first:
                        dve.wait_ge(s_p2, HC2 * (t - 1))
                    nc.vector.tensor_scalar(h1[:, b, c, :], ps_m[:, 1, 0:P], b1_sb[:, c:c + 1], 0.0,
                                            ALU.add, ALU.max).then_inc(s_h1_v, 1)
                dve.wait_ge(s_p2, HC2 * t + 2)
                nc.vector.tensor_scalar(h2[:, b, 1, :], ps_m[:, 1, 0:P], b2_sb[:, 1:2], 0.0,
                                        ALU.add, ALU.max).then_inc(s_h2_v, 1)

            both_tiles(dve, tile)

        @block.scalar
        def _(act):
            act.wait_ge(s_w2, 64)

            def tile(i, b, first):
                t = 2 * i + b
                for k in range(GROUPS):
                    if (GROUPS * b + k) % 2 == 1:
                        if not first:
                            act.wait_ge(s_p1, HC1 * (t - 1))
                        act.wait_ge(s_tr, t * GROUPS + k + 1)
                        if k == 0:
                            nc.scalar.copy(denseT[:, b, :], ps_t[:, GROUPS * b % 2, 0, :]).then_inc(s_dt, 1)
                        g = group_size(k)
                        nc.scalar.copy(
                            featT[:, b, :, GROUP * k:GROUP * k + g].rearrange("p s f -> p f s"),
                            ps_t[:, (GROUPS * b + k) % 2, 0:g, :]).then_inc(s_tr_a, 1)
                for u in range(UNITS):
                    act.wait_ge(s_gram, t * UNITS + u + 1)
                    for j in (2, 3):
                        for q in range(LANES):
                            nc.scalar.copy(*unit_move(b, u, j, q)).then_inc(s_gram_a, 1)
                for c in range(0, HC1, 2):
                    act.wait_ge(s_p1, HC1 * t + c + 1)
                    if not first:
                        act.wait_ge(s_p2, HC2 * (t - 1))
                    nc.scalar.activation(h1[:, b, c, :], ps_m[:, 0, 0:P], ACT.Relu,
                                         bias=b1_sb[:, c:c + 1]).then_inc(s_h1_a, 1)
                act.wait_ge(s_p2, HC2 * t + 1)
                nc.scalar.activation(h2[:, b, 0, :], ps_m[:, 0, 0:P], ACT.Relu,
                                     bias=b2_sb[:, 0:1]).then_inc(s_h2_a, 1)
                act.wait_ge(s_py, t + 1)
                nc.scalar.copy(y_sb[:, bass.ds(t, 1)], ps_m[:, 0, 0:1]).then_inc(s_y, 1)

            both_tiles(act, tile)

        @block.tensor
        def _(pe):
            pe.wait_ge(s_ident, 1)

            def transposes(i, b, first):
                t = 2 * i + b
                for k in range(GROUPS):
                    kk = GROUPS * b + k
                    if kk >= 2 or not first:
                        pe.wait_ge(s_tr_v if kk % 2 == 0 else s_tr_a, i * GROUPS + kk // 2)
                    if k == 2:
                        pe.wait_ge(s_dt, t + 1)
                    landed = group_size(k) - (k == 0)
                    if k == 0:
                        pe.wait_ge(s_dense[b], 16 * (i + 1))
                    pe.wait_ge(s_gather[b][k], 16 * landed * (i + 1))
                    for x in range(group_size(k)):
                        last = nc.tensor.transpose(ps_t[:, kk % 2, x, :], emb[:, b, GROUP * k + x, :], ident[:])
                    last.then_inc(s_tr, 1)

            def tile(i, b, first):
                t = 2 * i + b
                transposes(i, b, first)
                pe.wait_ge(s_tr_v, i * GROUPS + (GROUPS * b + GROUPS + 1) // 2)
                pe.wait_ge(s_tr_a, i * GROUPS + (GROUPS * b + GROUPS) // 2)
                for u in range(UNITS):
                    if u >= 2 or not (first and b == 0):
                        pe.wait_ge(s_gram_v, (t * UNITS + u - 1) * 2 * LANES)
                        pe.wait_ge(s_gram_a, (t * UNITS + u - 1) * 2 * LANES)
                    for g in range(UG):
                        s0 = (u * UG + g) * LANES
                        last = nc.tensor.matmul(ps_g[:, u % 2, g, 0:LANES * (N - 1)],
                                                featT[:, b, s0:s0 + LANES, :],
                                                featT[:, b, s0:s0 + LANES, 1:N], start=True, stop=True)
                    last.then_inc(s_gram, 1)
                if first and b == 0:
                    pe.wait_ge(s_wsum, 1)
                    pe.wait_ge(s_wp, 16 * len(pair_runs))
                    pe.wait_ge(s_w2, 64)
                pe.wait_ge(s_dt, t + 1)
                pe.wait_ge(s_gram_v, (t + 1) * UNITS * 2 * LANES)
                pe.wait_ge(s_gram_a, (t + 1) * UNITS * 2 * LANES)
                for c in range(HC1):
                    if c >= 2:
                        pe.wait_ge(s_h1_v if c % 2 else s_h1_a, HC1 // 2 * t + c // 2)
                    elif not (first and b == 0):
                        pe.wait_ge(s_h2_v if c % 2 else s_y, t)
                    cols = slice(c * P, (c + 1) * P)
                    nc.tensor.matmul(ps_m[:, c % 2, 0:P], w_dense[:, cols], denseT[:, b, :], start=True, stop=False)
                    for mm in range(MQ):
                        rows = rows_of_chunk(mm)
                        last = nc.tensor.matmul(ps_m[:, c % 2, 0:P], w_pair[0:rows, mm, cols], pairs[0:rows, b, mm, :],
                                                start=False, stop=(mm == MQ - 1))
                    last.then_inc(s_p1, 1)
                pe.wait_ge(s_h1_a, HC1 // 2 * (t + 1))
                pe.wait_ge(s_h1_v, HC1 // 2 * (t + 1))
                for c2 in range(HC2):
                    for c in range(HC1):
                        last = nc.tensor.matmul(ps_m[:, c2, 0:P], w2_sb[:, c, c2 * P:(c2 + 1) * P], h1[:, b, c, :],
                                                start=(c == 0), stop=(c == HC1 - 1))
                    last.then_inc(s_p2, 1)
                pe.wait_ge(s_h2_a, t + 1)
                pe.wait_ge(s_h2_v, t + 1)
                for c2 in range(HC2):
                    last = nc.tensor.matmul(ps_m[:, 0, 0:1], h2[:, b, c2, :], w3_sb[:, c2:c2 + 1],
                                            start=(c2 == 0), stop=(c2 == HC2 - 1))
                last.then_inc(s_py, 1)

            both_tiles(pe, tile)


_F = 26
_INS = (['r_dense_features', 'ids'] + [f'tbl_{f}' for f in range(_F)]
        + ['W_top1', 'b_top1', 'W_top2', 'b_top2', 'W_top3'])


def kernel(**inputs):
    import numpy as _np
    import concourse.bacc as _bacc
    from concourse import mybir as _mybir
    from concourse.bass_utils import run_bass_kernel_spmd as _run

    nc = _bacc.Bacc("TRN2", target_bir_lowering=False, num_devices=1)
    arrays, args = {}, []
    for name in _INS:
        a = _np.ascontiguousarray(inputs[name])
        arrays[f"in_{name}_dram"] = a
        args.append(nc.dram_tensor(f"in_{name}_dram", a.shape, _mybir.dt.from_np(a.dtype), kind="ExternalInput").ap())
    batch = inputs['r_dense_features'].shape[0]
    out = nc.dram_tensor("out_0_dram", (batch, 1), _mybir.dt.float32, kind="ExternalOutput").ap()
    dlrm_tower_kernel(nc, args[0], args[1], args[2:2 + _F], *args[2 + _F:], out)
    r = _run(nc, [arrays], core_ids=[0])
    return r.results[0]["out_0_dram"]
```

```python
import concourse.bass as bass
from concourse import mybir
from contextlib import ExitStack

P = 128
QUAD = 32


def dlrm_tower_kernel(nc, dense, ids, tables, W1, b1, W2, b2, W3, y):
    fp32, fp32r, fp16, i32 = mybir.dt.float32, mybir.dt.float32r, mybir.dt.float16, mybir.dt.int32
    ALU = mybir.AluOpType
    ACT = mybir.ActivationFunctionType

    B, D = dense.shape
    F = len(tables)
    N = F + 1
    H1, H2 = W2.shape
    TILES = B // P
    PAIRS = TILES // 2
    PAIR_ROWS = N * (N - 1) // 2
    LANES = P // QUAD
    MQ = -(-(N - 1) // LANES)
    UNITS = 4
    UG = P // LANES // UNITS
    BANK = 512
    HC1, HC2 = H1 // P, H2 // P

    LOOKUP = (13, 16, 19, 4, 11)
    GROUPS = ((0, 1, 2, 3), (5, 6, 7, 8), (20, 21, 22, 23), (9, 10, 14, 17), (12, 15, 18), (24, 25, 26))
    NG, GROUP, NL = len(GROUPS), len(GROUPS[0]), len(LOOKUP)
    assert sorted(LOOKUP + sum(GROUPS, ())) == list(range(N)) and GROUPS[0][0] == 0
    ROWS = tables[LOOKUP[0] - 1].shape[0]
    assert all(tables[n - 1].shape[0] == ROWS for n in LOOKUP)
    LC = -(-ROWS // P)
    LP = ROWS // LC
    assert LP * LC == ROWS
    JOBS = [(0, 1), (2,), (3,), (4,)]
    JOB_OF = {x: g for g, job in enumerate(JOBS) for x in job}
    SLOT = {x: job.index(x) for job in JOBS for x in job}
    assert sorted(JOB_OF) == list(range(NL))
    NJ = len(JOBS)
    SHARE = 8
    OHB = 4

    def runs(features):
        out, a = [], 0
        while a < len(features):
            e = a + 1
            step = features[e] - features[a] if e < len(features) else 1
            while e < len(features) and step > 0 and features[e] - features[e - 1] == step:
                e += 1
            out.append((a, features[a], features[e - 1] + 1, step if e > a + 1 else 1, e - a))
            a = e
        return out

    def columns(q):
        return min(MQ, N - 1 - MQ * q)

    def rows_of_chunk(mm):
        return QUAD * sum(mm < columns(q) for q in range(LANES))

    def pair_row(n, m):
        return D + n * (2 * N - n - 1) // 2 + (m - n - 1)

    pair_runs = []
    for n in range(N - 1):
        for q in range(LANES):
            lo = max(0, n - MQ * q)
            if lo < columns(q):
                pair_runs.append((n, lo, columns(q), q))

    def uses_of(jobs):
        first = [("T", 0, k) for k in range(NG)]
        second = [("T", 1, k) for k in range(NG)]
        if not jobs:
            return first + second
        return first + [("J", 0)] + second + [("J", g) for g in range(1, NJ)]

    PRO = [("J", g) for g in range(NJ)]
    STEADY = len(uses_of(True))
    assert len(PRO) % 2 == 0 and STEADY % 2 == 0

    ctx = ExitStack()
    with ctx:
        def sb(name, shape, dt=fp32):
            return ctx.enter_context(nc.sbuf_tensor(name, shape, dt))

        def pb(name, shape):
            return ctx.enter_context(nc.psum_tensor(name, shape, fp32))

        def sem(name):
            return ctx.enter_context(nc.semaphore(name))

        ident = sb("ident", [P, P])
        ident16 = sb("ident16", [P, P], fp16)
        w_dense = sb("w_dense", [D, H1])
        w_dense2 = sb("w_dense2", [D, H1])
        w_pair = sb("w_pair", [P, MQ, H1])
        w2_sb = sb("w2_sb", [P, HC1, H2])
        w3_sb = sb("w3_sb", [P, HC2])
        b1_sb = sb("b1_sb", [P, HC1])
        b2_sb = sb("b2_sb", [P, HC2])
        stage = sb("stage", [LP, 3, LC * D])
        tab_h = sb("tab_h", [LP, NL, LC, D])
        tab_l = sb("tab_l", [LP, NL, LC, D])
        row_i = sb("row_i", [LP, LC], i32)
        row = sb("row", [LP, LC])
        ids_all = sb("ids_all", [P, TILES, F], i32)
        ids16 = sb("ids16", [P, NL, TILES], fp16)
        onehot = sb("onehot", [LP, OHB, LC, 2 * P])
        stash = sb("stash", [D, NL, 2 * P])
        idx = sb("idx", [P, 2, F], i32)
        emb = sb("emb", [P, 2, NG, GROUP, D])
        featT = sb("featT", [D, 2, P, QUAD])
        denseT = sb("denseT", [D, 2, P])
        pairs = sb("pairs", [P, MQ, P])
        h1 = sb("h1", [P, HC1, P])
        h2 = sb("h2", [P, HC2, P])
        y_sb = sb("y_sb", [P, TILES])

        ps_t = pb("ps_t", [P, 2, BANK])
        ps_g = pb("ps_g", [P, 2, UG, P])
        ps_m = pb("ps_m", [P, BANK])
        ps_id = pb("ps_id", [P, 2, 2 * P])

        s_wd, s_wp, s_w2, s_ids = sem("s_wd"), sem("s_wp"), sem("s_w2"), sem("s_ids")
        s_stage = [sem(f"s_stage{x}") for x in range(3)]
        s_gather = [[sem(f"s_gather{b}_{k}") for k in range(NG)] for b in range(2)]
        s_idx = [sem(f"s_idx{b}") for b in range(2)]
        s_dense = [sem(f"s_dense{b}") for b in range(2)]
        s_open = sem("s_open")
        s_out = sem("s_out")
        s_zero, s_zero_feat, s_ident0, s_ident, s_ident16, s_row0, s_row, s_ids16, s_wsum = (
            sem(n) for n in ("s_zero", "s_zero_feat", "s_ident0", "s_ident", "s_ident16", "s_row0", "s_row",
                             "s_ids16", "s_wsum"))
        s_tab_h, s_tab_l = sem("s_tab_h"), sem("s_tab_l")
        s_tr, s_gram, s_p1, s_p2, s_py = (sem(n) for n in ("s_tr", "s_gram", "s_p1", "s_p2", "s_py"))
        s_id, s_looked = sem("s_id"), sem("s_looked")
        s_use_v, s_use_a, s_dt = sem("s_use_v"), sem("s_use_a"), sem("s_dt")
        s_onehot, s_placed = sem("s_onehot"), sem("s_placed")
        s_gram_v, s_gram_a = sem("s_gram_v"), sem("s_gram_a")
        s_h1, s_h2, s_y = sem("s_h1"), sem("s_h2"), sem("s_y")

        block = ctx.enter_context(nc.Block())
        dense_t = dense.rearrange("(p t) d -> t p d", t=TILES)
        ids_t = ids.rearrange("(p t) f -> t p f", t=TILES)

        def unit_move(u, j, q):
            c = columns(q)
            m0 = (N - 1) * j + MQ * q
            s0 = u * UG * LANES + j
            return (pairs[QUAD * q:QUAD * (q + 1), 0:c, s0:s0 + LANES * (UG - 1) + 1:LANES]
                    .rearrange("p m g -> p g m"),
                    ps_g[QUAD * j:QUAD * (j + 1), u % 2, :, m0:m0 + c])

        def group_moves(bank, b, k):
            return [(featT[:, b, :, f0:end:step].rearrange("p s f -> p f s"),
                     ps_t[:, bank, a * P:(a + n) * P].rearrange("p (f s) -> p f s", s=P))
                    for a, f0, end, step, n in runs(GROUPS[k])]

        def stash_moves(b):
            return [(featT[:, b, :, f0:end:step].rearrange("p s f -> p f s"),
                     stash[:, a:a + n, b * P:(b + 1) * P])
                    for a, f0, end, step, n in runs(LOOKUP)]

        def job_move(bank, g):
            n = len(JOBS[g])
            return (stash[:, JOBS[g][0]:JOBS[g][0] + n, :].rearrange("p x s -> p (x s)"),
                    ps_t[:, bank, 0:n * 2 * P])

        def all_pairs(eng, pair):
            pair(0, True, True)
            with eng.Fori(1, PAIRS - 1) as i:
                pair(i, False, True)
            pair(PAIRS - 1, False, False)

        def place(use, i, jobs):
            p = uses_of(jobs).index(use)
            return p % 2, len(PRO) // 2 + STEADY // 2 * i + p // 2

        def transposed(i, b, k):
            return (2 * i + b) * NG + k + 1

        def looked_up(g, r):
            return NL * r + JOBS[g][-1] + 1

        @block.sync
        def _(sp):
            def load_tile(i, b):
                sp.dma_start(idx[:, b, :], ids_t[2 * i + b]).then_inc(s_idx[b], 16)
                sp.dma_start(emb[:, b, 0, 0, :], dense_t[2 * i + b]).then_inc(s_dense[b], 16)

            def load_table(x):
                if x >= 3:
                    sp.wait_ge(s_tab_h, x - 2)
                    sp.wait_ge(s_tab_l, x - 2)
                sp.dma_start(stage[:, x % 3, :],
                             tables[LOOKUP[x] - 1].rearrange("(p c) d -> p (c d)", c=LC)).then_inc(s_stage[x % 3], 16)

            load_tile(0, 0)
            sp.dma_start(ids_all[:], ids.rearrange("(p t) f -> p t f", t=TILES)).then_inc(s_ids, 16)
            load_table(0)
            load_table(1)
            load_tile(0, 1)
            load_table(2)
            sp.dma_start(w_dense[:], W1[0:D, :]).then_inc(s_wd, 16)
            sp.dma_start(w_dense2[:], W1[D + PAIR_ROWS:D + PAIR_ROWS + D, :]).then_inc(s_wd, 16)
            sp.wait_ge(s_zero, 1)
            for z, (n, lo, hi, q) in enumerate(pair_runs):
                if z % SHARE == 0 and 3 + z // SHARE < NL:
                    load_table(3 + z // SHARE)
                r = pair_row(n, 1 + MQ * q + lo)
                part = QUAD * q + n
                sp.dma_start(w_pair[part:part + 1, lo:hi, :],
                             W1[r:r + hi - lo, :].rearrange("(a r) h -> a r h", a=1)).then_inc(s_wp, 16)
            sp.dma_start(w2_sb[:], W2.rearrange("(c p) n -> p c n", p=P)).then_inc(s_w2, 16)
            with nc.allow_non_contiguous_dma(reason="bias and last-layer vectors, 4 bytes a partition"):
                sp.dma_start(b1_sb[:], b1.rearrange("(c p) -> p c", p=P)).then_inc(s_w2, 16)
                sp.dma_start(b2_sb[:], b2.rearrange("(c p) -> p c", p=P)).then_inc(s_w2, 16)
                sp.dma_start(w3_sb[:], W3.rearrange("(c p) o -> p (c o)", p=P)).then_inc(s_w2, 16)

            def pair(i, jobs):
                for b in range(2):
                    sp.wait_ge(s_tr, transposed(i - 1, b, NG - 1))
                    load_tile(i, b)

            with sp.Fori(1, PAIRS) as i:
                pair(i, True)
            sp.wait_ge(s_y, TILES)
            sp.dma_start(y.rearrange("(p t) o -> p (t o)", t=TILES), y_sb[:]).then_inc(s_out, 16)
            sp.wait_ge(s_out, 16)

        @block.gpsimd
        def _(pool):
            pool.memset(ident[:], 0.0).then_inc(s_ident0, 1)
            pool.wait_ge(s_ident0, 1)
            pool.affine_select(out=ident[:], in_=ident[:], compare_op=ALU.not_equal, fill=1.0, base=0,
                               pattern=[[-1, P]], channel_multiplier=1).then_inc(s_ident, 1)
            pool.iota(row_i[:], pattern=[[1, LC]], base=0, channel_multiplier=LC).then_inc(s_row0, 1)
            pool.memset(w_pair[:], 0.0).then_inc(s_zero, 1)

            def tile(i, b):
                pool.wait_ge(s_idx[b], 16 * (i + 1))
                pool.sem_inc(s_open, 1)
                for k in range(NG):
                    for x, n in enumerate(GROUPS[k]):
                        if n:
                            pool.indirect_dma_start(
                                emb[:, b, k, x, :], None, tables[n - 1][:, :],
                                bass.IndirectOffsetOnAxis(ap=idx[:, b, n - 1:n], axis=0),
                            ).then_inc(s_gather[b][k], 16)

            for b in range(2):
                tile(0, b)
            with pool.Fori(1, PAIRS) as i:
                for b in range(2):
                    tile(i, b)

        @block.vector
        def _(dve):
            nc.vector.memset(featT[:, :, :, N:QUAD], 0.0).then_inc(s_zero_feat, 1)
            dve.wait_ge(s_row0, 1)
            nc.vector.tensor_copy(row[:], row_i[:]).then_inc(s_row, 1)
            dve.wait_ge(s_ident, 1)
            nc.vector.tensor_copy(ident16[:], ident[:]).then_inc(s_ident16, 1)
            dve.wait_ge(s_ids, 16)
            for x, n in enumerate(LOOKUP):
                nc.vector.tensor_copy(ids16[:, x, :], ids_all[:, :, n - 1]).then_inc(s_ids16, 1)
            dve.wait_ge(s_row, 1)

            def one_hots(x, r):
                dve.wait_ge(s_id, NJ * r + JOB_OF[x] + 1)
                before = NL * r + x - OHB + 1 if x >= OHB else NL * (r - 1) + (x + OHB if x + OHB < NL else x) + 1
                if x >= OHB or not (isinstance(r, int) and r == 0):
                    dve.wait_ge(s_looked, before)
                for c in range(LC):
                    last = nc.vector.tensor_scalar(onehot[:, x % OHB, c, :].bitcast(fp32r), ps_id[0:LP, SLOT[x], :],
                                                   row[:, c:c + 1], None, ALU.is_equal)
                last.then_inc(s_onehot, 1)

            def evacuate(use, i, jobs):
                bank, _ = place(use, i, jobs)
                if bank:
                    return
                if use[0] == "J":
                    dve.wait_ge(s_looked, looked_up(use[1], i + 1))
                    dve.wait_ge(s_placed, 2 * (i + 1))
                    nc.vector.tensor_copy(*job_move(0, use[1])).then_inc(s_use_v, 1)
                    return
                _, b, k = use
                dve.wait_ge(s_tr, transposed(i, b, k))
                if k == 0:
                    nc.vector.tensor_copy(denseT[:, b, :], ps_t[:, 0, 0:P]).then_inc(s_dt, 1)
                for move in group_moves(0, b, k):
                    last = nc.vector.tensor_copy(*move)
                last.then_inc(s_use_v, 1)

            def gram(i, b, units):
                t = 2 * i + b
                for u in units:
                    dve.wait_ge(s_gram, t * UNITS + u + 1)
                    for j in (0, 1):
                        for q in range(LANES):
                            last = nc.vector.tensor_copy(*unit_move(u, j, q))
                    last.then_inc(s_gram_v, 1)

            for g in range(NJ):
                for x in JOBS[g]:
                    one_hots(x, 0)
                for x in JOBS[g]:
                    dve.wait_ge(s_stage[x % 3], 16 * (x // 3 + 1))
                    dve.wait_ge(s_tab_h, x + 1)
                    nc.vector.tensor_tensor(tab_l[:, x].rearrange("p c d -> p (c d)").bitcast(fp32r), stage[:, x % 3, :],
                                            tab_h[:, x].rearrange("p c d -> p (c d)"), ALU.subtract).then_inc(s_tab_l, 1)
                if g % 2:
                    dve.wait_ge(s_looked, looked_up(g - 1, 0))
                    nc.vector.tensor_copy(*job_move(0, g - 1)).then_inc(s_use_v, 1)
            dve.wait_ge(s_wd, 32)
            nc.vector.tensor_tensor(w_dense[:], w_dense[:], w_dense2[:], ALU.add).then_inc(s_wsum, 1)

            def evacuate_tile(i, b, jobs, g):
                for k in range(NG):
                    evacuate(("T", b, k), i, jobs)
                    if jobs and k % 2 == 0 and k // 2 < len(JOBS[g]):
                        one_hots(JOBS[g][k // 2], i + 1)

            def pair(i, first, jobs):
                evacuate_tile(i, 0, jobs, 0)
                if jobs:
                    one_hots(JOBS[1][0], i + 1)
                    evacuate(("J", 0), i, jobs)
                    for x in JOBS[1][1:]:
                        one_hots(x, i + 1)
                gram(i, 0, range(UNITS))
                evacuate_tile(i, 1, jobs, 2)
                if jobs:
                    evacuate(("J", 1), i, jobs)
                    for x in JOBS[3]:
                        one_hots(x, i + 1)
                gram(i, 1, (0, 1))
                if jobs:
                    evacuate(("J", 2), i, jobs)
                gram(i, 1, (2, 3))
                if jobs:
                    evacuate(("J", 3), i, jobs)

            all_pairs(dve, pair)

        @block.scalar
        def _(act):
            for x in range(NL):
                act.wait_ge(s_stage[x % 3], 16 * (x // 3 + 1))
                nc.scalar.copy(tab_h[:, x].rearrange("p c d -> p (c d)").bitcast(fp32r),
                               stage[:, x % 3, :]).then_inc(s_tab_h, 1)
                if x == JOBS[2][-1]:
                    act.wait_ge(s_looked, looked_up(1, 0))
                    nc.scalar.copy(*job_move(1, 1)).then_inc(s_use_a, 1)
            act.wait_ge(s_looked, looked_up(3, 0))
            nc.scalar.copy(*job_move(1, 3)).then_inc(s_use_a, 1)
            def evacuate(use, i, jobs):
                bank, _ = place(use, i, jobs)
                if not bank:
                    return
                if use[0] == "J":
                    act.wait_ge(s_looked, looked_up(use[1], i + 1))
                    act.wait_ge(s_placed, 2 * (i + 1))
                    nc.scalar.copy(*job_move(1, use[1])).then_inc(s_use_a, 1)
                    return
                _, b, k = use
                act.wait_ge(s_tr, transposed(i, b, k))
                if k == 0:
                    nc.scalar.copy(denseT[:, b, :], ps_t[:, 1, 0:P]).then_inc(s_dt, 1)
                for move in group_moves(1, b, k):
                    last = nc.scalar.copy(*move)
                last.then_inc(s_use_a, 1)

            def gram(i, b, units):
                t = 2 * i + b
                for u in units:
                    act.wait_ge(s_gram, t * UNITS + u + 1)
                    for j in (2, 3):
                        for q in range(LANES):
                            last = nc.scalar.copy(*unit_move(u, j, q))
                    last.then_inc(s_gram_a, 1)

            def relu1(t):
                act.wait_ge(s_p1, t + 1)
                for c in range(HC1):
                    last = nc.scalar.activation(h1[:, c, :], ps_m[:, c * P:(c + 1) * P], ACT.Relu,
                                                bias=b1_sb[:, c:c + 1])
                last.then_inc(s_h1, 1)

            def relu2(t):
                act.wait_ge(s_p2, t + 1)
                for c in range(HC2):
                    last = nc.scalar.activation(h2[:, c, :], ps_m[:, c * P:(c + 1) * P], ACT.Relu,
                                                bias=b2_sb[:, c:c + 1])
                last.then_inc(s_h2, 1)

            def take_y(t):
                act.wait_ge(s_py, t + 1)
                nc.scalar.copy(y_sb[:, bass.ds(t, 1)], ps_m[:, HC2 * P:HC2 * P + 1]).then_inc(s_y, 1)

            def pair(i, first, jobs):
                act.wait_ge(s_use_v, len(PRO) // 2 + STEADY // 2 * i)
                act.wait_ge(s_use_a, len(PRO) // 2 + STEADY // 2 * i)
                if not first:
                    act.wait_ge(s_gram, 2 * i * UNITS)
                evacuate(("T", 0, 0), i, jobs)
                evacuate(("T", 0, 1), i, jobs)
                for b in range(2):
                    for move in stash_moves(b):
                        last = nc.scalar.copy(*move)
                    last.then_inc(s_placed, 1)
                for k in range(2, NG):
                    evacuate(("T", 0, k), i, jobs)
                if not first:
                    relu1(2 * i - 1)
                    relu2(2 * i - 1)
                if jobs:
                    evacuate(("J", 0), i, jobs)
                if not first:
                    take_y(2 * i - 1)
                gram(i, 0, range(UNITS))
                for k in range(NG):
                    evacuate(("T", 1, k), i, jobs)
                if first:
                    act.wait_ge(s_w2, 64)
                relu1(2 * i)
                relu2(2 * i)
                if jobs:
                    evacuate(("J", 1), i, jobs)
                take_y(2 * i)
                gram(i, 1, (0, 1))
                if jobs:
                    evacuate(("J", 2), i, jobs)
                gram(i, 1, (2, 3))
                if jobs:
                    evacuate(("J", 3), i, jobs)

            all_pairs(act, pair)
            relu1(TILES - 1)
            relu2(TILES - 1)
            take_y(TILES - 1)

        @block.tensor
        def _(pe):
            pe.wait_ge(s_ident16, 1)
            pe.wait_ge(s_ids16, NL)

            def spread_ids(g, r):
                if g >= 1 or not (isinstance(r, int) and r == 0):
                    pe.wait_ge(s_onehot, NL * r + JOBS[g][0])
                for x in JOBS[g]:
                    for b in range(2):
                        last = nc.tensor.matmul(ps_id[:, SLOT[x], b * P:(b + 1) * P],
                                                ids16[:, x, bass.ds(2 * r + b, 1)].to_broadcast([P, P]),
                                                ident16[:], start=True, stop=True)
                last.then_inc(s_id, 1)

            def lookup(g, r, bank, freed, some=(0, 1)):
                if some[0] == 0 and not (isinstance(freed, int) and freed == 0):
                    pe.wait_ge(s_use_a if bank else s_use_v, freed)
                for x in JOBS[g][some[0]:some[-1] + 1]:
                    if isinstance(r, int) and r == 0:
                        pe.wait_ge(s_tab_h, x + 1)
                        pe.wait_ge(s_tab_l, x + 1)
                    pe.wait_ge(s_onehot, NL * r + x + 1)
                    out = ps_t[:, bank, SLOT[x] * 2 * P:(SLOT[x] + 1) * 2 * P]
                    for c in range(LC):
                        for part in (tab_h, tab_l):
                            last = nc.tensor.matmul(out, part[:, x, c, :].bitcast(fp32r),
                                                    onehot[:, x % OHB, c, :].bitcast(fp32r),
                                                    start=(c == 0 and part is tab_h),
                                                    stop=(c == LC - 1 and part is tab_l))
                    last.then_inc(s_looked, 1)

            def job(g, i, some=(0, 1)):
                bank, freed = place(("J", g), i, True)
                lookup(g, i + 1, bank, freed, some)

            def transposes(i, b, jobs, groups):
                for k in groups:
                    bank, freed = place(("T", b, k), i, jobs)
                    pe.wait_ge(s_use_a if bank else s_use_v, freed)
                    if k == 0:
                        pe.wait_ge(s_dense[b], 16 * (i + 1))
                    pe.wait_ge(s_gather[b][k], 16 * (len(GROUPS[k]) - (k == 0)) * (i + 1))
                    for x in range(len(GROUPS[k])):
                        last = nc.tensor.transpose(ps_t[:, bank, x * P:(x + 1) * P], emb[:, b, k, x, :], ident[:])
                    last.then_inc(s_tr, 1)

            def gram(i, b, units, jobs):
                t = 2 * i + b
                if units[0] == 0:
                    for k in (NG - 2, NG - 1):
                        bank, freed = place(("T", b, k), i, jobs)
                        pe.wait_ge(s_use_a if bank else s_use_v, freed + 1)
                    pe.wait_ge(s_placed, t + 1)
                    if isinstance(t, int) and t == 0:
                        pe.wait_ge(s_zero_feat, 1)
                for u in units:
                    if not isinstance(t, int) or t * UNITS + u >= 2:
                        pe.wait_ge(s_gram_v, t * UNITS + u - 1)
                        pe.wait_ge(s_gram_a, t * UNITS + u - 1)
                    for g in range(UG):
                        s0 = (u * UG + g) * LANES
                        last = nc.tensor.matmul(ps_g[:, u % 2, g, 0:LANES * (N - 1)],
                                                featT[:, b, s0:s0 + LANES, :],
                                                featT[:, b, s0:s0 + LANES, 1:N], start=True, stop=True)
                    last.then_inc(s_gram, 1)

            def layer1_ready(t):
                if isinstance(t, int) and t == 0:
                    pe.wait_ge(s_wsum, 1)
                    pe.wait_ge(s_wp, 16 * len(pair_runs))
                    pe.wait_ge(s_w2, 64)
                else:
                    pe.wait_ge(s_y, t)
                pe.wait_ge(s_dt, t + 1)
                pe.wait_ge(s_gram_v, (t + 1) * UNITS)
                pe.wait_ge(s_gram_a, (t + 1) * UNITS)

            def layer1(b, c):
                cols = slice(c * P, (c + 1) * P)
                nc.tensor.matmul(ps_m[:, cols], w_dense[:, cols], denseT[:, b, :], start=True, stop=False)
                for mm in range(MQ):
                    rows = rows_of_chunk(mm)
                    last = nc.tensor.matmul(ps_m[:, cols], w_pair[0:rows, mm, cols], pairs[0:rows, mm, :],
                                            start=False, stop=(mm == MQ - 1))
                if c == HC1 - 1:
                    last.then_inc(s_p1, 1)

            def layer1_and_transposes(t, i, b, jobs):
                transposes(i, b, jobs, (0, 1))
                layer1_ready(t)
                for c in range(HC1):
                    layer1(1 - b, c)
                    if c + 2 < NG:
                        transposes(i, b, jobs, (c + 2,))

            def layer2(t):
                pe.wait_ge(s_h1, t + 1)
                for c2 in range(HC2):
                    for c in range(HC1):
                        last = nc.tensor.matmul(ps_m[:, c2 * P:(c2 + 1) * P], w2_sb[:, c, c2 * P:(c2 + 1) * P],
                                                h1[:, c, :], start=(c == 0), stop=(c == HC1 - 1))
                last.then_inc(s_p2, 1)

            def layer3(t):
                pe.wait_ge(s_h2, t + 1)
                for c2 in range(HC2):
                    last = nc.tensor.matmul(ps_m[:, HC2 * P:HC2 * P + 1], h2[:, c2, :], w3_sb[:, c2:c2 + 1],
                                            start=(c2 == 0), stop=(c2 == HC2 - 1))
                last.then_inc(s_py, 1)

            spread_ids(0, 0)
            for g in range(NJ):
                if g + 1 < NJ:
                    spread_ids(g + 1, 0)
                lookup(g, 0, g % 2, g // 2)

            def pair(i, first, jobs):
                if jobs:
                    spread_ids(0, i + 1)
                if first:
                    transposes(i, 0, jobs, range(NG))
                else:
                    layer1_and_transposes(2 * i - 1, i, 0, jobs)
                if jobs:
                    job(0, i, (0,))
                    spread_ids(1, i + 1)
                if not first:
                    layer2(2 * i - 1)
                if jobs:
                    job(0, i, (1,))
                if not first:
                    layer3(2 * i - 1)
                gram(i, 0, range(UNITS), jobs)
                if jobs:
                    spread_ids(2, i + 1)
                layer1_and_transposes(2 * i, i, 1, jobs)
                if jobs:
                    job(1, i, (0,))
                    spread_ids(3, i + 1)
                layer2(2 * i)
                if jobs:
                    job(1, i, (1,))
                layer3(2 * i)
                gram(i, 1, (0, 1), jobs)
                if jobs:
                    job(2, i)
                gram(i, 1, (2, 3), jobs)
                if jobs:
                    job(3, i)

            all_pairs(pe, pair)
            layer1_ready(TILES - 1)
            for c in range(HC1):
                layer1(1, c)
            layer2(TILES - 1)
            layer3(TILES - 1)


_F = 26
_INS = (['r_dense_features', 'ids'] + [f'tbl_{f}' for f in range(_F)]
        + ['W_top1', 'b_top1', 'W_top2', 'b_top2', 'W_top3'])


def kernel(**inputs):
    import numpy as _np
    import concourse.bacc as _bacc
    from concourse import mybir as _mybir
    from concourse.bass_utils import run_bass_kernel_spmd as _run

    nc = _bacc.Bacc("TRN2", target_bir_lowering=False, num_devices=1)
    arrays, args = {}, []
    for name in _INS:
        a = _np.ascontiguousarray(inputs[name])
        arrays[f"in_{name}_dram"] = a
        args.append(nc.dram_tensor(f"in_{name}_dram", a.shape, _mybir.dt.from_np(a.dtype), kind="ExternalInput").ap())
    batch = inputs['r_dense_features'].shape[0]
    out = nc.dram_tensor("out_0_dram", (batch, 1), _mybir.dt.float32, kind="ExternalOutput").ap()
    dlrm_tower_kernel(nc, args[0], args[1], args[2:2 + _F], *args[2 + _F:], out)
    r = _run(nc, [arrays], core_ids=[0])
    return r.results[0]["out_0_dram"]
```

```python
import concourse.bass as bass
from concourse import mybir
from contextlib import ExitStack

P = 128
QUAD = 32


def dlrm_tower_kernel(nc, dense, ids, tables, W1, b1, W2, b2, W3, y):
    fp32, fp32r, fp16, i32 = mybir.dt.float32, mybir.dt.float32r, mybir.dt.float16, mybir.dt.int32
    ALU = mybir.AluOpType
    ACT = mybir.ActivationFunctionType

    B, D = dense.shape
    F = len(tables)
    N = F + 1
    H1, H2 = W2.shape
    TILES = B // P
    PAIRS = TILES // 2
    PAIR_ROWS = N * (N - 1) // 2
    LANES = P // QUAD
    MQ = -(-(N - 1) // LANES)
    Z = MQ + 1
    UNITS = 4
    UG = P // LANES // UNITS
    BANK = 512
    HC1, HC2 = H1 // P, H2 // P

    LOOKUP = (13, 16, 19, 4, 11)
    GROUPS = ((0, 1, 2, 3), (5, 6, 7, 8), (20, 21, 22, 23), (9, 10, 14, 17), (12, 15, 18), (24, 25, 26))
    NG, GROUP, NL = len(GROUPS), len(GROUPS[0]), len(LOOKUP)
    assert sorted(LOOKUP + sum(GROUPS, ())) == list(range(N)) and GROUPS[0][0] == 0
    ROWS = tables[LOOKUP[0] - 1].shape[0]
    assert all(tables[n - 1].shape[0] == ROWS for n in LOOKUP)
    LC = -(-ROWS // P)
    LP = ROWS // LC
    assert LP * LC == ROWS
    JOBS = [(0, 1), (2,), (3,), (4,)]
    JOB_OF = {x: g for g, job in enumerate(JOBS) for x in job}
    SLOT = {x: job.index(x) for job in JOBS for x in job}
    assert sorted(JOB_OF) == list(range(NL))
    NJ = len(JOBS)
    NEXT = 38
    SHARE = 5
    OHB = 4
    BY_DVE, BY_ACT, BUFFER0 = (0, 2, 4), (1, 3), (0, 1, 2, 3, 2)
    assert sorted(BY_DVE + BY_ACT) == list(range(NL)) and len(BY_DVE) == 3 and len(BY_ACT) == 2

    def runs(features):
        out, a = [], 0
        while a < len(features):
            e = a + 1
            step = features[e] - features[a] if e < len(features) else 1
            while e < len(features) and step > 0 and features[e] - features[e - 1] == step:
                e += 1
            out.append((a, features[a], features[e - 1] + 1, step if e > a + 1 else 1, e - a))
            a = e
        return out

    def columns(q):
        return min(MQ, N - 1 - MQ * q)

    def pair_row(n, m):
        return D + n * (2 * N - n - 1) // 2 + (m - n - 1)

    pair_runs = []
    for n in range(N - 1):
        for q in range(LANES):
            lo = max(0, n - MQ * q)
            if pair_runs and lo == 0 and columns(q) == MQ and pair_runs[-1][:3] == (n, 0, MQ):
                last = pair_runs[-1]
                pair_runs[-1] = (n, 0, MQ, last[3], last[4] + 1)
            elif lo < columns(q):
                pair_runs.append((n, lo, columns(q), q, 1))

    def uses_of(jobs):
        first = [("T", 0, k) for k in range(NG)]
        second = [("T", 1, k) for k in range(NG)]
        if not jobs:
            return first + second
        return first + [("J", 0)] + second + [("J", g) for g in range(1, NJ)]

    PRO = [("J", g) for g in range(NJ)]
    STEADY = len(uses_of(True))
    assert len(PRO) % 2 == 0 and STEADY % 2 == 0

    ctx = ExitStack()
    with ctx:
        def sb(name, shape, dt=fp32):
            return ctx.enter_context(nc.sbuf_tensor(name, shape, dt))

        def pb(name, shape):
            return ctx.enter_context(nc.psum_tensor(name, shape, fp32))

        def sem(name):
            return ctx.enter_context(nc.semaphore(name))

        ident = sb("ident", [P, P])
        ident16 = sb("ident16", [P, P], fp16)
        w_dense = sb("w_dense", [D, H1])
        w_dense2 = sb("w_dense2", [D, H1])
        w1_h = sb("w1_h", [P, Z, H1])
        w1_l = sb("w1_l", [P, Z, H1])
        w2_sb = sb("w2_sb", [P, HC1, H2])
        w3_sb = sb("w3_sb", [P, HC2])
        b1_sb = sb("b1_sb", [P, HC1])
        b2_sb = sb("b2_sb", [P, HC2])
        early = sb("early", [P, 3 * LC * D])
        stage = early[0:LP, :].rearrange("p (x c) -> p x c", x=3)
        tab_h = sb("tab_h", [LP, NL, LC, D])
        tab_l = sb("tab_l", [LP, NL, LC, D])
        row_i = sb("row_i", [LP, LC], i32)
        row = sb("row", [LP, LC])
        minus_row = sb("minus_row", [LP, LC])
        ids_all = sb("ids_all", [P, TILES, F], i32)
        ids16 = sb("ids16", [P, NL, TILES], fp16)
        onehot = sb("onehot", [LP, OHB, LC, 2 * P])
        stash = sb("stash", [D, NL, 2 * P])
        idx = sb("idx", [P, 2, F], i32)
        emb = sb("emb", [P, 2, NG, GROUP, D])
        featT = sb("featT", [D, 2, P, QUAD])
        z_raw = early[:, 0:Z * 2 * P].rearrange("p (z s) -> p z s", z=Z)
        z_h = sb("z_h", [P, Z, 2 * P])
        z_l = sb("z_l", [P, Z, 2 * P])
        h1 = early[:, Z * 2 * P:(Z + HC1) * 2 * P].rearrange("p (c s) -> p c s", c=HC1)
        h2 = sb("h2", [P, HC2, 2 * P])
        w_pair = featT[:, 1].rearrange("p s f -> p (s f)")[:, 0:MQ * H1].rearrange("p (m h) -> p m h", m=MQ)
        y_sb = sb("y_sb", [P, TILES])

        ps_t = pb("ps_t", [P, 2, BANK])
        ps_g = pb("ps_g", [P, 2, UG, P])
        ps_m = pb("ps_m", [P, BANK])
        ps_id = pb("ps_id", [P, 2, 2 * P])

        s_wd, s_wp, s_w2, s_ids = sem("s_wd"), sem("s_wp"), sem("s_w2"), sem("s_ids")
        s_stage = [sem(f"s_stage{x}") for x in range(3)]
        s_gather = [[sem(f"s_gather{b}_{k}") for k in range(NG)] for b in range(2)]
        s_idx = [sem(f"s_idx{b}") for b in range(2)]
        s_dense = [sem(f"s_dense{b}") for b in range(2)]
        s_open = sem("s_open")
        s_gathered = sem("s_gathered")
        s_out = sem("s_out")
        s_zero, s_zero_feat, s_ident0, s_ident, s_ident16, s_row0, s_row, s_ids16, s_wsum = (
            sem(n) for n in ("s_zero", "s_zero_feat", "s_ident0", "s_ident", "s_ident16", "s_row0", "s_row",
                             "s_ids16", "s_wsum"))
        s_w1_h, s_w1_l, s_zero_z = sem("s_w1_h"), sem("s_w1_l"), sem("s_zero_z")
        s_tab_h, s_tab_l = sem("s_tab_h"), sem("s_tab_l")
        s_tr, s_gram, s_p1, s_p2, s_py = (sem(n) for n in ("s_tr", "s_gram", "s_p1", "s_p2", "s_py"))
        s_id, s_looked = sem("s_id"), sem("s_looked")
        s_id0_v, s_id0_a = sem("s_id0_v"), sem("s_id0_a")
        s_use_v, s_use_a, s_dt = sem("s_use_v"), sem("s_use_a"), sem("s_dt")
        s_onehot, s_placed = sem("s_onehot"), sem("s_placed")
        s_onehot0_v, s_onehot0_a, s_distance = sem("s_onehot0_v"), sem("s_onehot0_a"), sem("s_distance")
        s_minus_row = sem("s_minus_row")
        s_gram_v, s_gram_a = sem("s_gram_v"), sem("s_gram_a")
        s_z_h, s_z_l = sem("s_z_h"), sem("s_z_l")
        s_h1, s_h2, s_y = sem("s_h1"), sem("s_h2"), sem("s_y")

        block = ctx.enter_context(nc.Block())
        dense_t = dense.rearrange("(p t) d -> t p d", t=TILES)
        ids_t = ids.rearrange("(p t) f -> t p f", t=TILES)

        def unit_move(b, u, j, q):
            c = columns(q)
            m0 = (N - 1) * j + MQ * q
            s0 = b * P + u * UG * LANES + j
            return (z_raw[QUAD * q:QUAD * (q + 1), 0:c, s0:s0 + LANES * (UG - 1) + 1:LANES]
                    .rearrange("p m g -> p g m"),
                    ps_g[QUAD * j:QUAD * (j + 1), u % 2, :, m0:m0 + c])

        def group_moves(bank, b, k):
            return [(featT[:, b, :, f0:end:step].rearrange("p s f -> p f s"),
                     ps_t[:, bank, a * P:(a + n) * P].rearrange("p (f s) -> p f s", s=P))
                    for a, f0, end, step, n in runs(GROUPS[k])]

        def stash_moves(b):
            return [(featT[:, b, :, f0:end:step].rearrange("p s f -> p f s"),
                     stash[:, a:a + n, b * P:(b + 1) * P])
                    for a, f0, end, step, n in runs(LOOKUP)]

        def job_move(bank, g):
            n = len(JOBS[g])
            return (stash[:, JOBS[g][0]:JOBS[g][0] + n, :].rearrange("p x s -> p (x s)"),
                    ps_t[:, bank, 0:n * 2 * P])

        def all_pairs(eng, pair):
            pair(0, True, True)
            with eng.Fori(1, PAIRS - 1) as i:
                pair(i, False, True)
            pair(PAIRS - 1, False, False)

        def place(use, i, jobs):
            p = uses_of(jobs).index(use)
            return p % 2, len(PRO) // 2 + STEADY // 2 * i + p // 2

        def gathers(k):
            return sum(n > 0 for n in GROUPS[k])

        def transposed(i, b, k):
            return (2 * i + b) * NG + k + 1

        def looked_up(g, r):
            return NL * r + JOBS[g][-1] + 1

        def out1(i, c):
            half, slot = divmod(c, HC1 // 2)
            bank = ps_t[:, half, :] if final(i) else ps_m
            return bank[:, slot * 2 * P:(slot + 1) * 2 * P]

        def out2(i, c):
            if final(i) and c:
                return ps_g[:, 0, 0:2, :].rearrange("p a s -> p (a s)")
            return ps_m[:, c * 2 * P:(c + 1) * 2 * P]

        def ids0(x):
            if x == BY_DVE[2]:
                return ps_g[:, 0, 0:2, :].rearrange("p a s -> p (a s)")
            if x in BY_DVE:
                return ps_id[:, BY_DVE.index(x), :]
            slot = BY_ACT.index(x)
            return ps_m[:, slot * 2 * P:(slot + 1) * 2 * P]

        def final(i):
            return isinstance(i, int) and i == PAIRS - 1

        def z_raw_free(eng, i, b):
            if isinstance(i, int) and i == 0:
                eng.wait_ge(s_tab_h, NL)
                eng.wait_ge(s_tab_l, NL)
            else:
                eng.wait_ge(s_z_h, 2 * i + b - 1)
                eng.wait_ge(s_z_l, 2 * i + b - 1)

        @block.sync
        def _(sp):
            def load_idx(i, b):
                if not isinstance(i, int) or i:
                    for k in range(NG):
                        sp.wait_ge(s_gather[b][k], 16 * gathers(k) * i)
                        sp.sem_inc(s_gathered, 1)
                sp.dma_start(idx[:, b, :], ids_t[2 * i + b]).then_inc(s_idx[b], 16)

            def load_dense(i, b):
                if not isinstance(i, int) or i:
                    sp.wait_ge(s_tr, transposed(i - 1, b, NG - 1))
                sp.dma_start(emb[:, b, 0, 0, :], dense_t[2 * i + b]).then_inc(s_dense[b], 16)

            def load_table(x):
                if x >= 3:
                    sp.wait_ge(s_tab_h, x - 2)
                    sp.wait_ge(s_tab_l, x - 2)
                sp.dma_start(stage[:, x % 3, :],
                             tables[LOOKUP[x] - 1].rearrange("(p c) d -> p (c d)", c=LC)).then_inc(s_stage[x % 3], 16)

            load_idx(0, 0)
            load_dense(0, 0)
            sp.dma_start(ids_all[:], ids.rearrange("(p t) f -> p t f", t=TILES)).then_inc(s_ids, 16)
            load_table(0)
            load_table(1)
            load_idx(0, 1)
            load_dense(0, 1)
            load_table(2)
            sp.dma_start(w_dense[:], W1[0:D, :]).then_inc(s_wd, 16)
            sp.dma_start(w_dense2[:], W1[D + PAIR_ROWS:D + PAIR_ROWS + D, :]).then_inc(s_wd, 16)
            sp.wait_ge(s_zero, 2)
            for z, (n, lo, hi, q, count) in enumerate(pair_runs):
                if z and z % SHARE == 0 and 2 + z // SHARE < NL:
                    load_table(2 + z // SHARE)
                if z == NEXT:
                    load_idx(1, 0)
                r = pair_row(n, 1 + MQ * q + lo)
                part = QUAD * q + n
                sp.dma_start(w_pair[part:part + QUAD * (count - 1) + 1:QUAD, lo:hi, :],
                             W1[r:r + (hi - lo) * count, :].rearrange("(a r) h -> a r h", a=count)
                             ).then_inc(s_wp, 16)
            sp.dma_start(w2_sb[:], W2.rearrange("(c p) n -> p c n", p=P)).then_inc(s_w2, 16)
            with nc.allow_non_contiguous_dma(reason="bias and last-layer vectors, 4 bytes a partition"):
                sp.dma_start(b1_sb[:], b1.rearrange("(c p) -> p c", p=P)).then_inc(s_w2, 16)
                sp.dma_start(b2_sb[:], b2.rearrange("(c p) -> p c", p=P)).then_inc(s_w2, 16)
                sp.dma_start(w3_sb[:], W3.rearrange("(c p) o -> p (c o)", p=P)).then_inc(s_w2, 16)

            load_dense(1, 0)
            with sp.Fori(1, PAIRS - 1) as i:
                load_idx(i, 1)
                load_dense(i, 1)
                load_idx(i + 1, 0)
                load_dense(i + 1, 0)
            load_idx(PAIRS - 1, 1)
            load_dense(PAIRS - 1, 1)
            sp.wait_ge(s_y, PAIRS)
            sp.dma_start(y.rearrange("(p t) o -> p (t o)", t=TILES), y_sb[:]).then_inc(s_out, 16)
            sp.wait_ge(s_out, 16)

        @block.gpsimd
        def _(pool):
            pool.memset(ident[:], 0.0).then_inc(s_ident0, 1)
            pool.wait_ge(s_ident0, 1)
            pool.affine_select(out=ident[:], in_=ident[:], compare_op=ALU.not_equal, fill=1.0, base=0,
                               pattern=[[-1, P]], channel_multiplier=1).then_inc(s_ident, 1)
            pool.iota(row_i[:], pattern=[[1, LC]], base=0, channel_multiplier=LC).then_inc(s_row0, 1)
            pool.memset(w_pair[:, MQ // 2 + 1:MQ], 0.0).then_inc(s_zero, 1)

            def tile(i, b):
                if not isinstance(i, int) or i:
                    pool.wait_ge(s_tr, transposed(i - 1, b, NG - 1))
                pool.wait_ge(s_idx[b], 16 * (i + 1))
                pool.sem_inc(s_open, 1)
                for k in range(NG):
                    for x, n in enumerate(GROUPS[k]):
                        if n:
                            pool.indirect_dma_start(
                                emb[:, b, k, x, :], None, tables[n - 1][:, :],
                                bass.IndirectOffsetOnAxis(ap=idx[:, b, n - 1:n], axis=0),
                            ).then_inc(s_gather[b][k], 16)

            for b in range(2):
                tile(0, b)
            with pool.Fori(1, PAIRS) as i:
                for b in range(2):
                    tile(i, b)

        @block.vector
        def _(dve):
            nc.vector.memset(featT[:, 0, :, N:QUAD], 0.0).then_inc(s_zero_feat, 1)
            dve.wait_ge(s_row0, 1)
            nc.vector.tensor_copy(row[:], row_i[:]).then_inc(s_row, 1)
            dve.wait_ge(s_ident, 1)
            nc.vector.tensor_copy(ident16[:], ident[:]).then_inc(s_ident16, 1)
            nc.vector.memset(w_pair[:, 0:MQ // 2 + 1], 0.0).then_inc(s_zero, 1)
            dve.wait_ge(s_ids, 16)
            for x, n in enumerate(LOOKUP):
                nc.vector.tensor_copy(ids16[:, x, :], ids_all[:, :, n - 1]).then_inc(s_ids16, 1)
            dve.wait_ge(s_row, 1)
            nc.vector.tensor_scalar(minus_row[:], row[:], -1.0, None, ALU.mult).then_inc(s_minus_row, 1)

            def equal(x, buffer, numbers):
                for c in range(LC):
                    last = nc.vector.tensor_scalar(onehot[:, buffer, c, :].bitcast(fp32r), numbers,
                                                   row[:, c:c + 1], None, ALU.is_equal)
                return last

            def one_hots0(x):
                dve.wait_ge(s_id0_v, 1)
                if BUFFER0.index(BUFFER0[x]) != x:
                    dve.wait_ge(s_looked, BUFFER0.index(BUFFER0[x]) + 1)
                equal(x, BUFFER0[x], ids0(x)[0:LP]).then_inc(s_onehot0_v, 1)

            def table_rest(x):
                dve.wait_ge(s_tab_h, x + 1)
                nc.vector.tensor_tensor(tab_l[:, x].rearrange("p c d -> p (c d)").bitcast(fp32r), stage[:, x % 3, :],
                                        tab_h[:, x].rearrange("p c d -> p (c d)"), ALU.subtract).then_inc(s_tab_l, 1)

            def evacuate0(g):
                dve.wait_ge(s_looked, looked_up(g, 0))
                nc.vector.tensor_copy(*job_move(0, g)).then_inc(s_use_v, 1)

            def one_hots(x, r):
                dve.wait_ge(s_id, NJ * (r - 1) + JOB_OF[x] + 1)
                if isinstance(r, int) and r == 1 and x < OHB:
                    dve.wait_ge(s_looked, max(y for y in range(NL) if BUFFER0[y] == x) + 1)
                else:
                    dve.wait_ge(s_looked, NL * r + x - OHB + 1 if x >= OHB else
                                NL * (r - 1) + (x + OHB if x + OHB < NL else x) + 1)
                equal(x, x % OHB, ps_id[0:LP, SLOT[x], :]).then_inc(s_onehot, 1)

            def evacuate(use, i, jobs):
                bank, _ = place(use, i, jobs)
                if bank:
                    return
                if use[0] == "J":
                    dve.wait_ge(s_looked, looked_up(use[1], i + 1))
                    dve.wait_ge(s_placed, 2 * (i + 1))
                    nc.vector.tensor_copy(*job_move(0, use[1])).then_inc(s_use_v, 1)
                    return
                _, b, k = use
                dve.wait_ge(s_tr, transposed(i, b, k))
                if k == 0:
                    z_raw_free(dve, i, b)
                    nc.vector.tensor_copy(z_raw[:, MQ, b * P:(b + 1) * P], ps_t[:, 0, 0:P]).then_inc(s_dt, 1)
                for move in group_moves(0, b, k):
                    last = nc.vector.tensor_copy(*move)
                last.then_inc(s_use_v, 1)

            def gram(i, b, units):
                t = 2 * i + b
                if units[0] == 0:
                    z_raw_free(dve, i, b)
                for u in units:
                    dve.wait_ge(s_gram, t * UNITS + u + 1)
                    for j in (0, 1):
                        for q in range(LANES):
                            last = nc.vector.tensor_copy(*unit_move(b, u, j, q))
                    last.then_inc(s_gram_v, 1)

            def split(i, b):
                cols = slice(b * P, (b + 1) * P)
                dve.wait_ge(s_z_h, 2 * i + b + 1)
                nc.vector.tensor_tensor(z_l[:, :, cols].bitcast(fp32r), z_raw[:, :, cols], z_h[:, :, cols],
                                        ALU.subtract).then_inc(s_z_l, 1)

            def prepare_layer1():
                dve.wait_ge(s_tab_l, NL)
                for mm in range(MQ):
                    for q in range(LANES):
                        if mm == columns(q):
                            nc.vector.memset(z_raw[QUAD * q:QUAD * (q + 1), mm:MQ, :], 0.0).then_inc(s_zero_z, 1)
                dve.wait_ge(s_wd, 32)
                nc.vector.tensor_tensor(w_dense[:], w_dense[:], w_dense2[:], ALU.add).then_inc(s_wsum, 1)

            def split_weights():
                dve.wait_ge(s_wsum, 1)
                dve.wait_ge(s_w1_h, 2)
                nc.vector.tensor_tensor(w1_l[:, MQ, :].bitcast(fp32r), w_dense[:], w1_h[:, MQ, :], ALU.subtract)
                nc.vector.tensor_tensor(w1_l[:, 0:MQ, :].bitcast(fp32r), w_pair, w1_h[:, 0:MQ, :],
                                        ALU.subtract).then_inc(s_w1_l, 1)
                dve.wait_ge(s_w1_l, 1)
                nc.vector.memset(featT[:, 1, :, N:QUAD], 0.0).then_inc(s_zero_feat, 1)

            one_hots0(0)
            table_rest(0)
            table_rest(1)
            one_hots0(2)
            table_rest(2)
            evacuate0(0)
            table_rest(3)
            one_hots0(4)
            table_rest(4)
            for x in JOBS[0]:
                one_hots(x, 1)
                if x == JOBS[0][0]:
                    evacuate0(2)

            def pair(i, first, jobs):
                evacuate(("T", 0, 0), i, jobs)
                evacuate(("T", 0, 1), i, jobs)
                if jobs and not first:
                    one_hots(JOBS[0][0], i + 1)
                evacuate(("T", 0, 2), i, jobs)
                evacuate(("T", 0, 3), i, jobs)
                if jobs and not first:
                    one_hots(JOBS[0][1], i + 1)
                evacuate(("T", 0, 4), i, jobs)
                evacuate(("T", 0, 5), i, jobs)
                if first:
                    prepare_layer1()
                if jobs:
                    one_hots(JOBS[1][0], i + 1)
                    if not first:
                        evacuate(("J", 0), i, jobs)
                        one_hots(JOBS[2][0], i + 1)
                gram(i, 0, (0, 1))
                if first:
                    split_weights()
                gram(i, 0, (2, 3))
                if first:
                    evacuate(("J", 0), i, jobs)
                for k in range(NG):
                    evacuate(("T", 1, k), i, jobs)
                if jobs:
                    one_hots(JOBS[2 if first else 3][0], i + 1)
                split(i, 0)
                gram(i, 1, (0, 1))
                if first:
                    one_hots(JOBS[3][0], i + 1)
                gram(i, 1, (2, 3))
                if jobs:
                    evacuate(("J", 2), i, jobs)
                split(i, 1)

            all_pairs(dve, pair)

        @block.scalar
        def _(act):
            def round_table(x):
                act.wait_ge(s_stage[x % 3], 16 * (x // 3 + 1))
                nc.scalar.copy(tab_h[:, x].rearrange("p c d -> p (c d)").bitcast(fp32r),
                               stage[:, x % 3, :]).then_inc(s_tab_h, 1)

            def one_hots0(x):
                turn = BY_ACT.index(x)
                act.wait_ge(s_id0_a, 1)
                act.wait_ge(s_minus_row, 1)
                for c in range(LC):
                    last = nc.scalar.activation(onehot[:, BUFFER0[x], c, :].bitcast(fp32r), ids0(x)[0:LP], ACT.Abs,
                                                bias=minus_row[:, c:c + 1])
                last.then_inc(s_distance, 1)
                act.wait_ge(s_distance, turn + 1)
                whole = onehot[:, BUFFER0[x]].rearrange("p c s -> p (c s)")
                nc.scalar.activation(whole.bitcast(fp32r), whole, ACT.Relu, bias=1.0, scale=-1.0).then_inc(s_onehot0_a, 1)

            def evacuate0(g):
                act.wait_ge(s_looked, looked_up(g, 0))
                nc.scalar.copy(*job_move(1, g)).then_inc(s_use_a, 1)

            for x in range(3):
                round_table(x)
            one_hots0(1)
            for x in range(3, NL):
                round_table(x)
            one_hots0(3)
            evacuate0(1)
            evacuate0(3)

            def evacuate(use, i, jobs):
                bank, _ = place(use, i, jobs)
                if not bank:
                    return
                if use[0] == "J":
                    act.wait_ge(s_looked, looked_up(use[1], i + 1))
                    act.wait_ge(s_placed, 2 * (i + 1))
                    nc.scalar.copy(*job_move(1, use[1])).then_inc(s_use_a, 1)
                    return
                _, b, k = use
                act.wait_ge(s_tr, transposed(i, b, k))
                if k == 0:
                    z_raw_free(act, i, b)
                    nc.scalar.copy(z_raw[:, MQ, b * P:(b + 1) * P], ps_t[:, 1, 0:P]).then_inc(s_dt, 1)
                for move in group_moves(1, b, k):
                    last = nc.scalar.copy(*move)
                last.then_inc(s_use_a, 1)

            def gram(i, b, units):
                t = 2 * i + b
                if units[0] == 0:
                    z_raw_free(act, i, b)
                for u in units:
                    act.wait_ge(s_gram, t * UNITS + u + 1)
                    for j in (2, 3):
                        for q in range(LANES):
                            last = nc.scalar.copy(*unit_move(b, u, j, q))
                    last.then_inc(s_gram_a, 1)

            def move_stash(b):
                for move in stash_moves(b):
                    last = nc.scalar.copy(*move)
                last.then_inc(s_placed, 1)

            def round_weights():
                act.wait_ge(s_wsum, 1)
                nc.scalar.copy(w1_h[:, MQ, :].bitcast(fp32r), w_dense[:]).then_inc(s_w1_h, 1)
                act.wait_ge(s_wp, 16 * len(pair_runs))
                nc.scalar.copy(w1_h[:, 0:MQ, :].bitcast(fp32r), w_pair).then_inc(s_w1_h, 1)

            def split(i, b):
                t = 2 * i + b
                cols = slice(b * P, (b + 1) * P)
                if isinstance(i, int) and i == 0:
                    act.wait_ge(s_zero_z, 1)
                else:
                    act.wait_ge(s_p1, 2 * i)
                act.wait_ge(s_dt, t + 1)
                act.wait_ge(s_gram_v, (t + 1) * UNITS)
                act.wait_ge(s_gram_a, (t + 1) * UNITS)
                nc.scalar.copy(z_h[:, :, cols].bitcast(fp32r), z_raw[:, :, cols]).then_inc(s_z_h, 1)

            def relu1(i, half):
                act.wait_ge(s_p1, 2 * i + half + 1)
                for c in range(HC1 // 2):
                    c1 = HC1 // 2 * half + c
                    last = nc.scalar.activation(h1[:, c1, :], out1(i, c1), ACT.Relu,
                                                bias=b1_sb[:, c1:c1 + 1])
                last.then_inc(s_h1, 1)

            def relu2(i):
                act.wait_ge(s_p2, i + 1)
                for c in range(HC2):
                    last = nc.scalar.activation(h2[:, c, :], out2(i, c), ACT.Relu,
                                                bias=b2_sb[:, c:c + 1])
                last.then_inc(s_h2, 1)

            def take_y(i):
                act.wait_ge(s_py, i + 1)
                nc.scalar.copy(y_sb[:, bass.ds(2 * i, 2)], ps_m[:, 0:2]).then_inc(s_y, 1)

            def pair(i, first, jobs):
                act.wait_ge(s_use_v, len(PRO) // 2 + STEADY // 2 * i)
                act.wait_ge(s_use_a, len(PRO) // 2 + STEADY // 2 * i)
                if not first:
                    act.wait_ge(s_gram, 2 * i * UNITS)
                evacuate(("T", 0, 0), i, jobs)
                evacuate(("T", 0, 1), i, jobs)
                move_stash(0)
                if not first:
                    move_stash(1)
                for k in range(2, NG - 1):
                    evacuate(("T", 0, k), i, jobs)
                if not first:
                    relu1(i - 1, 0)
                evacuate(("T", 0, NG - 1), i, jobs)
                if not first:
                    relu1(i - 1, 1)
                if first:
                    round_weights()
                gram(i, 0, range(UNITS))
                if first:
                    act.wait_ge(s_w1_l, 1)
                    move_stash(1)
                for k in range(NG):
                    evacuate(("T", 1, k), i, jobs)
                split(i, 0)
                if not first and jobs:
                    relu2(i - 1)
                if jobs:
                    evacuate(("J", 1), i, jobs)
                if first:
                    act.wait_ge(s_w2, 64)
                elif jobs:
                    take_y(i - 1)
                gram(i, 1, range(UNITS))
                split(i, 1)
                if jobs:
                    evacuate(("J", 3), i, jobs)
                else:
                    relu2(i - 1)
                    take_y(i - 1)

            all_pairs(act, pair)
            for half in range(2):
                relu1(PAIRS - 1, half)
            relu2(PAIRS - 1)
            take_y(PAIRS - 1)

        @block.tensor
        def _(pe):
            pe.wait_ge(s_ident16, 1)
            pe.wait_ge(s_ids16, NL)

            def spread_ids(g, r):
                if g == 0 and isinstance(r, int) and r == 1:
                    pe.wait_ge(s_onehot0_v, len(BY_DVE))
                else:
                    pe.wait_ge(s_onehot, NL * (r - 1) + JOBS[g][0])
                for x in JOBS[g]:
                    for b in range(2):
                        last = nc.tensor.matmul(ps_id[:, SLOT[x], b * P:(b + 1) * P],
                                                ids16[:, x, bass.ds(2 * r + b, 1)].to_broadcast([P, P]),
                                                ident16[:], start=True, stop=True)
                last.then_inc(s_id, 1)

            def spread_ids0(lookups, done):
                for x in lookups:
                    for b in range(2):
                        last = nc.tensor.matmul(ids0(x)[:, b * P:(b + 1) * P], ids16[:, x, b:b + 1].to_broadcast([P, P]),
                                                ident16[:], start=True, stop=True)
                last.then_inc(done, 1)

            def lookup(g, r, bank, freed):
                if not (isinstance(freed, int) and freed == 0):
                    pe.wait_ge(s_use_a if bank else s_use_v, freed)
                for x in JOBS[g]:
                    if isinstance(r, int) and r == 0:
                        pe.wait_ge(s_tab_h, x + 1)
                        pe.wait_ge(s_tab_l, x + 1)
                        if x in BY_DVE:
                            pe.wait_ge(s_onehot0_v, BY_DVE.index(x) + 1)
                        else:
                            pe.wait_ge(s_onehot0_a, BY_ACT.index(x) + 1)
                        buffer = BUFFER0[x]
                    else:
                        pe.wait_ge(s_onehot, NL * (r - 1) + x + 1)
                        buffer = x % OHB
                    out = ps_t[:, bank, SLOT[x] * 2 * P:(SLOT[x] + 1) * 2 * P]
                    for c in range(LC):
                        for part in (tab_h, tab_l):
                            last = nc.tensor.matmul(out, part[:, x, c, :].bitcast(fp32r),
                                                    onehot[:, buffer, c, :].bitcast(fp32r),
                                                    start=(c == 0 and part is tab_h),
                                                    stop=(c == LC - 1 and part is tab_l))
                    last.then_inc(s_looked, 1)

            def job(g, i):
                bank, freed = place(("J", g), i, True)
                lookup(g, i + 1, bank, freed)

            def transposes(i, b, jobs, groups):
                for k in groups:
                    bank, freed = place(("T", b, k), i, jobs)
                    pe.wait_ge(s_use_a if bank else s_use_v, freed)
                    if k == 0:
                        pe.wait_ge(s_dense[b], 16 * (i + 1))
                    pe.wait_ge(s_gather[b][k], 16 * gathers(k) * (i + 1))
                    for x in range(len(GROUPS[k])):
                        last = nc.tensor.transpose(ps_t[:, bank, x * P:(x + 1) * P], emb[:, b, k, x, :], ident[:])
                    last.then_inc(s_tr, 1)

            def gram(i, b, units, jobs):
                t = 2 * i + b
                if units[0] == 0:
                    for k in (NG - 2, NG - 1):
                        bank, freed = place(("T", b, k), i, jobs)
                        pe.wait_ge(s_use_a if bank else s_use_v, freed + 1)
                    pe.wait_ge(s_placed, t + 1)
                    if isinstance(t, int) and t < 2:
                        pe.wait_ge(s_zero_feat, t + 1)
                for u in units:
                    if not isinstance(t, int) or t * UNITS + u >= 2:
                        pe.wait_ge(s_gram_v, t * UNITS + u - 1)
                        pe.wait_ge(s_gram_a, t * UNITS + u - 1)
                    for g in range(UG):
                        s0 = (u * UG + g) * LANES
                        last = nc.tensor.matmul(ps_g[:, u % 2, g, 0:LANES * (N - 1)],
                                                featT[:, b, s0:s0 + LANES, :],
                                                featT[:, b, s0:s0 + LANES, 1:N], start=True, stop=True)
                    last.then_inc(s_gram, 1)

            def layer1(i, c):
                half, slot = divmod(c, HC1 // 2)
                if slot == 0:
                    if final(i):
                        pe.wait_ge(s_use_v, len(PRO) // 2 + (STEADY * (PAIRS - 1) + 2 * NG) // 2)
                        pe.wait_ge(s_use_a, len(PRO) // 2 + (STEADY * (PAIRS - 1) + 2 * NG) // 2)
                    elif half:
                        pe.wait_ge(s_h1, 2 * i + 1)
                    elif not isinstance(i, int) or i:
                        pe.wait_ge(s_y, i)
                if c == 0:
                    pe.wait_ge(s_z_h, 2 * i + 2)
                cols = slice(c * P, (c + 1) * P)
                products = [(w, z_h, zz) for zz in range(Z) for w in (w1_h, w1_l)] + [(w1_h, z_l, zz) for zz in range(Z)]
                for k, (w, z, zz) in enumerate(products):
                    if c == 0 and k == 2 * Z:
                        pe.wait_ge(s_z_l, 2 * i + 2)
                    last = nc.tensor.matmul(out1(i, c), w[:, zz, cols].bitcast(fp32r),
                                            z[:, zz, :].bitcast(fp32r),
                                            start=(k == 0), stop=(k == len(products) - 1))
                if slot == HC1 // 2 - 1:
                    last.then_inc(s_p1, 1)

            def layer2(i, c2, some=range(HC1)):
                if c2 == 0 and not final(i):
                    pe.wait_ge(s_h1, 2 * i + 2)
                for c in some:
                    last = nc.tensor.matmul(out2(i, c2), w2_sb[:, c, c2 * P:(c2 + 1) * P],
                                            h1[:, c, :], start=(c == 0), stop=(c == HC1 - 1))
                if c2 == HC2 - 1 and some[-1] == HC1 - 1:
                    last.then_inc(s_p2, 1)

            def layer3(i):
                pe.wait_ge(s_h2, i + 1)
                for b in range(2):
                    for c2 in range(HC2):
                        last = nc.tensor.matmul(ps_m[:, b:b + 1], h2[:, c2, b * P:(b + 1) * P], w3_sb[:, c2:c2 + 1],
                                                start=(c2 == 0), stop=(c2 == HC2 - 1))
                last.then_inc(s_py, 1)

            spread_ids0(BY_DVE, s_id0_v)
            spread_ids0(BY_ACT, s_id0_a)
            for g in range(NJ):
                if g == NJ - 2:
                    spread_ids(0, 1)
                lookup(g, 0, g % 2, g // 2)

            def pair(i, first, jobs):
                if jobs and not first:
                    spread_ids(0, i + 1)
                transposes(i, 0, jobs, (0, 1))
                if not first:
                    layer1(i - 1, 0)
                transposes(i, 0, jobs, (2, 3))
                if not first:
                    layer1(i - 1, 1)
                transposes(i, 0, jobs, range(4, NG))
                if not first:
                    layer1(i - 1, 2)
                if jobs:
                    spread_ids(1, i + 1)
                    job(0, i)
                    if not first:
                        spread_ids(2, i + 1)
                if not first:
                    layer1(i - 1, 3)
                gram(i, 0, range(UNITS), jobs)
                if jobs:
                    spread_ids(2 if first else 3, i + 1)
                transposes(i, 1, jobs, (0, 1))
                if not first:
                    layer2(i - 1, 0)
                transposes(i, 1, jobs, (2, 3))
                if not first:
                    layer2(i - 1, 1, range(HC1 // 2))
                transposes(i, 1, jobs, range(4, NG))
                if not first and jobs:
                    layer2(i - 1, 1, range(HC1 // 2, HC1))
                if jobs:
                    job(1, i)
                if not first and jobs:
                    layer3(i - 1)
                gram(i, 1, (0, 1), jobs)
                if first:
                    spread_ids(3, i + 1)
                gram(i, 1, (2, 3), jobs)
                if jobs:
                    job(2, i)
                    job(3, i)
                if first:
                    pe.wait_ge(s_w1_h, 2)
                    pe.wait_ge(s_w1_l, 1)
                    pe.wait_ge(s_w2, 64)

            all_pairs(pe, pair)
            layer2(PAIRS - 2, 1, range(HC1 // 2, HC1))
            layer1(PAIRS - 1, 0)
            layer3(PAIRS - 2)
            for c in range(1, HC1):
                layer1(PAIRS - 1, c)
            pe.wait_ge(s_y, PAIRS - 1)
            pe.wait_ge(s_gram_v, TILES * UNITS)
            pe.wait_ge(s_gram_a, TILES * UNITS)
            for c in range(HC1):
                if c % (HC1 // 2) == 0:
                    pe.wait_ge(s_h1, 2 * (PAIRS - 1) + c // (HC1 // 2) + 1)
                for c2 in range(HC2):
                    layer2(PAIRS - 1, c2, (c,))
            layer3(PAIRS - 1)


_F = 26
_INS = (['r_dense_features', 'ids'] + [f'tbl_{f}' for f in range(_F)]
        + ['W_top1', 'b_top1', 'W_top2', 'b_top2', 'W_top3'])


def kernel(**inputs):
    import numpy as _np
    import concourse.bacc as _bacc
    from concourse import mybir as _mybir
    from concourse.bass_utils import run_bass_kernel_spmd as _run

    nc = _bacc.Bacc("TRN2", target_bir_lowering=False, num_devices=1)
    arrays, args = {}, []
    for name in _INS:
        a = _np.ascontiguousarray(inputs[name])
        arrays[f"in_{name}_dram"] = a
        args.append(nc.dram_tensor(f"in_{name}_dram", a.shape, _mybir.dt.from_np(a.dtype), kind="ExternalInput").ap())
    batch = inputs['r_dense_features'].shape[0]
    out = nc.dram_tensor("out_0_dram", (batch, 1), _mybir.dt.float32, kind="ExternalOutput").ap()
    dlrm_tower_kernel(nc, args[0], args[1], args[2:2 + _F], *args[2 + _F:], out)
    r = _run(nc, [arrays], core_ids=[0])
    return r.results[0]["out_0_dram"]
```
